# Optimizing a Trainium2 kernel written in Bass

```python
import numpy as np
import jax
import jax.numpy as jnp

def _softmax(x, axis=-1):
    return jax.nn.softmax(x, axis=axis)

def _gelu(x):
    return jax.nn.gelu(x, approximate=True)

def _silu(x):
    return jax.nn.silu(x)

def _sigmoid(x):
    return jax.nn.sigmoid(x)

def _layernorm(x, axis=-1, eps=1e-05):
    m = jnp.mean(x, axis=axis, keepdims=True)
    v = jnp.var(x, axis=axis, keepdims=True)
    return (x - m) / jnp.sqrt(v + eps)

def _scatter_add(tgt, idx, src, axis=0):
    return tgt.at[idx].add(src)

def _segment_sum(src, seg, n):
    return jax.ops.segment_sum(src, seg, n)
kernel_name = 'mk_dlrm_tower_d1_rec_r8_ed173d'

def setup_inputs(seed: int=0):
    np.random.seed(seed)
    _w = jnp.asarray

    def _rec_inputs():
        import jax
        import jax.numpy as jnp
        _tk = jax.random.key(seed)
        dense_ctx = jax.random.normal(jax.random.fold_in(_tk, 190), (512, 16), jnp.float32)
        ids = jnp.stack([jax.random.randint(jax.random.fold_in(_tk, 200 + f), (512,), 0, v, jnp.int32) for f, v in enumerate([12500, 1000, 12500, 1000, 12500, 1000, 1250, 12500, 1250, 1000, 1250, 125000, 12500, 1250, 125000, 12500, 12500, 1000, 1250, 1000, 12500, 1000, 12500, 1000, 1000, 1250, 12500, 1250, 1250, 1000, 125000, 125000, 12500, 12500, 1250, 125000, 125000, 1250, 1000, 1250])], axis=1)
        tbl_0 = 0.05 * jax.random.normal(jax.random.fold_in(_tk, 500 + 0), (12500, 32), jnp.float32)
        tbl_1 = 0.05 * jax.random.normal(jax.random.fold_in(_tk, 500 + 1), (1000, 32), jnp.float32)
        tbl_2 = 0.05 * jax.random.normal(jax.random.fold_in(_tk, 500 + 2), (12500, 32), jnp.float32)
        tbl_3 = 0.05 * jax.random.normal(jax.random.fold_in(_tk, 500 + 3), (1000, 32), jnp.float32)
        tbl_4 = 0.05 * jax.random.normal(jax.random.fold_in(_tk, 500 + 4), (12500, 32), jnp.float32)
        tbl_5 = 0.05 * jax.random.normal(jax.random.fold_in(_tk, 500 + 5), (1000, 32), jnp.float32)
        tbl_6 = 0.05 * jax.random.normal(jax.random.fold_in(_tk, 500 + 6), (1250, 32), jnp.float32)
        tbl_7 = 0.05 * jax.random.normal(jax.random.fold_in(_tk, 500 + 7), (12500, 32), jnp.float32)
        tbl_8 = 0.05 * jax.random.normal(jax.random.fold_in(_tk, 500 + 8), (1250, 32), jnp.float32)
        tbl_9 = 0.05 * jax.random.normal(jax.random.fold_in(_tk, 500 + 9), (1000, 32), jnp.float32)
        tbl_10 = 0.05 * jax.random.normal(jax.random.fold_in(_tk, 500 + 10), (1250, 32), jnp.float32)
        tbl_11 = 0.05 * jax.random.normal(jax.random.fold_in(_tk, 500 + 11), (125000, 32), jnp.float32)
        tbl_12 = 0.05 * jax.random.normal(jax.random.fold_in(_tk, 500 + 12), (12500, 32), jnp.float32)
        tbl_13 = 0.05 * jax.random.normal(jax.random.fold_in(_tk, 500 + 13), (1250, 32), jnp.float32)
        tbl_14 = 0.05 * jax.random.normal(jax.random.fold_in(_tk, 500 + 14), (125000, 32), jnp.float32)
        tbl_15 = 0.05 * jax.random.normal(jax.random.fold_in(_tk, 500 + 15), (12500, 32), jnp.float32)
        tbl_16 = 0.05 * jax.random.normal(jax.random.fold_in(_tk, 500 + 16), (12500, 32), jnp.float32)
        tbl_17 = 0.05 * jax.random.normal(jax.random.fold_in(_tk, 500 + 17), (1000, 32), jnp.float32)
        tbl_18 = 0.05 * jax.random.normal(jax.random.fold_in(_tk, 500 + 18), (1250, 32), jnp.float32)
        tbl_19 = 0.05 * jax.random.normal(jax.random.fold_in(_tk, 500 + 19), (1000, 32), jnp.float32)
        tbl_20 = 0.05 * jax.random.normal(jax.random.fold_in(_tk, 500 + 20), (12500, 32), jnp.float32)
        tbl_21 = 0.05 * jax.random.normal(jax.random.fold_in(_tk, 500 + 21), (1000, 32), jnp.float32)
        tbl_22 = 0.05 * jax.random.normal(jax.random.fold_in(_tk, 500 + 22), (12500, 32), jnp.float32)
        tbl_23 = 0.05 * jax.random.normal(jax.random.fold_in(_tk, 500 + 23), (1000, 32), jnp.float32)
        tbl_24 = 0.05 * jax.random.normal(jax.random.fold_in(_tk, 500 + 24), (1000, 32), jnp.float32)
        tbl_25 = 0.05 * jax.random.normal(jax.random.fold_in(_tk, 500 + 25), (1250, 32), jnp.float32)
        tbl_26 = 0.05 * jax.random.normal(jax.random.fold_in(_tk, 500 + 26), (12500, 32), jnp.float32)
        tbl_27 = 0.05 * jax.random.normal(jax.random.fold_in(_tk, 500 + 27), (1250, 32), jnp.float32)
        tbl_28 = 0.05 * jax.random.normal(jax.random.fold_in(_tk, 500 + 28), (1250, 32), jnp.float32)
        tbl_29 = 0.05 * jax.random.normal(jax.random.fold_in(_tk, 500 + 29), (1000, 32), jnp.float32)
        tbl_30 = 0.05 * jax.random.normal(jax.random.fold_in(_tk, 500 + 30), (125000, 32), jnp.float32)
        tbl_31 = 0.05 * jax.random.normal(jax.random.fold_in(_tk, 500 + 31), (125000, 32), jnp.float32)
        tbl_32 = 0.05 * jax.random.normal(jax.random.fold_in(_tk, 500 + 32), (12500, 32), jnp.float32)
        tbl_33 = 0.05 * jax.random.normal(jax.random.fold_in(_tk, 500 + 33), (12500, 32), jnp.float32)
        tbl_34 = 0.05 * jax.random.normal(jax.random.fold_in(_tk, 500 + 34), (1250, 32), jnp.float32)
        tbl_35 = 0.05 * jax.random.normal(jax.random.fold_in(_tk, 500 + 35), (125000, 32), jnp.float32)
        tbl_36 = 0.05 * jax.random.normal(jax.random.fold_in(_tk, 500 + 36), (125000, 32), jnp.float32)
        tbl_37 = 0.05 * jax.random.normal(jax.random.fold_in(_tk, 500 + 37), (1250, 32), jnp.float32)
        tbl_38 = 0.05 * jax.random.normal(jax.random.fold_in(_tk, 500 + 38), (1000, 32), jnp.float32)
        tbl_39 = 0.05 * jax.random.normal(jax.random.fold_in(_tk, 500 + 39), (1250, 32), jnp.float32)
        _rk = jax.random.fold_in(_tk, 7)
        W_top1 = 0.0354441 * jax.random.normal(jax.random.fold_in(_tk, 801), (796, 512), jnp.float32)
        W_top2 = 0.0441942 * jax.random.normal(jax.random.fold_in(_tk, 802), (512, 256), jnp.float32)
        W_top3 = 0.0625 * jax.random.normal(jax.random.fold_in(_tk, 803), (256, 1), jnp.float32)
        b_top1 = jnp.zeros((512,), jnp.float32)
        b_top2 = jnp.zeros((256,), jnp.float32)
        return (dense_ctx, ids, tbl_0, tbl_1, tbl_2, tbl_3, tbl_4, tbl_5, tbl_6, tbl_7, tbl_8, tbl_9, tbl_10, tbl_11, tbl_12, tbl_13, tbl_14, tbl_15, tbl_16, tbl_17, tbl_18, tbl_19, tbl_20, tbl_21, tbl_22, tbl_23, tbl_24, tbl_25, tbl_26, tbl_27, tbl_28, tbl_29, tbl_30, tbl_31, tbl_32, tbl_33, tbl_34, tbl_35, tbl_36, tbl_37, tbl_38, tbl_39, W_top1, b_top1, W_top2, b_top2, W_top3)
    dense_ctx, ids, tbl_0, tbl_1, tbl_2, tbl_3, tbl_4, tbl_5, tbl_6, tbl_7, tbl_8, tbl_9, tbl_10, tbl_11, tbl_12, tbl_13, tbl_14, tbl_15, tbl_16, tbl_17, tbl_18, tbl_19, tbl_20, tbl_21, tbl_22, tbl_23, tbl_24, tbl_25, tbl_26, tbl_27, tbl_28, tbl_29, tbl_30, tbl_31, tbl_32, tbl_33, tbl_34, tbl_35, tbl_36, tbl_37, tbl_38, tbl_39, W_top1, b_top1, W_top2, b_top2, W_top3 = _rec_inputs()

    def _L0_rec_setup():
        import jax, jax.numpy as jnp
        import numpy as np
        NUM_FIELDS = 40
        EMBED_DIM = 32
        BATCH = 512
        NUM_PAIRS = NUM_FIELDS * (NUM_FIELDS - 1) // 2
        key = jax.random.key(seed)
        k1, k2 = jax.random.split(key)
        inputs = jax.random.normal(k1, (BATCH, NUM_FIELDS, EMBED_DIM), dtype=jnp.float32)
        std = (2.0 / (EMBED_DIM + EMBED_DIM)) ** 0.5
        bilinear_matrices = jax.random.normal(k2, (NUM_PAIRS, EMBED_DIM, EMBED_DIM), dtype=jnp.float32) * std
        return {'inputs': inputs, 'bilinear_matrices': bilinear_matrices}
    _L0_rec_all = _L0_rec_setup()
    _L0_rec_in = {k: v for k, v in _L0_rec_all.items() if k in ('bilinear_matrices',)}
    del _L0_rec_all
    return {'dense_ctx': dense_ctx, 'ids': ids, 'tbl_0': tbl_0, 'tbl_1': tbl_1, 'tbl_2': tbl_2, 'tbl_3': tbl_3, 'tbl_4': tbl_4, 'tbl_5': tbl_5, 'tbl_6': tbl_6, 'tbl_7': tbl_7, 'tbl_8': tbl_8, 'tbl_9': tbl_9, 'tbl_10': tbl_10, 'tbl_11': tbl_11, 'tbl_12': tbl_12, 'tbl_13': tbl_13, 'tbl_14': tbl_14, 'tbl_15': tbl_15, 'tbl_16': tbl_16, 'tbl_17': tbl_17, 'tbl_18': tbl_18, 'tbl_19': tbl_19, 'tbl_20': tbl_20, 'tbl_21': tbl_21, 'tbl_22': tbl_22, 'tbl_23': tbl_23, 'tbl_24': tbl_24, 'tbl_25': tbl_25, 'tbl_26': tbl_26, 'tbl_27': tbl_27, 'tbl_28': tbl_28, 'tbl_29': tbl_29, 'tbl_30': tbl_30, 'tbl_31': tbl_31, 'tbl_32': tbl_32, 'tbl_33': tbl_33, 'tbl_34': tbl_34, 'tbl_35': tbl_35, 'tbl_36': tbl_36, 'tbl_37': tbl_37, 'tbl_38': tbl_38, 'tbl_39': tbl_39, 'W_top1': W_top1, 'b_top1': b_top1, 'W_top2': W_top2, 'b_top2': b_top2, 'W_top3': W_top3, 'L0_rec_bilinear_matrices': _L0_rec_in['bilinear_matrices']}

def reference(dense_ctx, ids, tbl_0, tbl_1, tbl_2, tbl_3, tbl_4, tbl_5, tbl_6, tbl_7, tbl_8, tbl_9, tbl_10, tbl_11, tbl_12, tbl_13, tbl_14, tbl_15, tbl_16, tbl_17, tbl_18, tbl_19, tbl_20, tbl_21, tbl_22, tbl_23, tbl_24, tbl_25, tbl_26, tbl_27, tbl_28, tbl_29, tbl_30, tbl_31, tbl_32, tbl_33, tbl_34, tbl_35, tbl_36, tbl_37, tbl_38, tbl_39, W_top1, b_top1, W_top2, b_top2, W_top3, L0_rec_bilinear_matrices):
    import jax
    import jax.numpy as jnp

    def _L0_rec_ref(inputs, bilinear_matrices):
        import jax, jax.numpy as jnp
        import numpy as np
        NUM_FIELDS = 40
        EMBED_DIM = 32
        BATCH = 512
        NUM_PAIRS = NUM_FIELDS * (NUM_FIELDS - 1) // 2
        num_fields = inputs.shape[1]
        iidx, jidx = jnp.triu_indices(num_fields, k=1)
        xi = inputs[:, iidx, :]
        xj = inputs[:, jidx, :]
        out = jnp.einsum('bpd,pde,bpe->bp', xi, bilinear_matrices, xj)
        return out
    e = jnp.stack([tbl_0[ids[:, 0]], tbl_1[ids[:, 1]], tbl_2[ids[:, 2]], tbl_3[ids[:, 3]], tbl_4[ids[:, 4]], tbl_5[ids[:, 5]], tbl_6[ids[:, 6]], tbl_7[ids[:, 7]], tbl_8[ids[:, 8]], tbl_9[ids[:, 9]], tbl_10[ids[:, 10]], tbl_11[ids[:, 11]], tbl_12[ids[:, 12]], tbl_13[ids[:, 13]], tbl_14[ids[:, 14]], tbl_15[ids[:, 15]], tbl_16[ids[:, 16]], tbl_17[ids[:, 17]], tbl_18[ids[:, 18]], tbl_19[ids[:, 19]], tbl_20[ids[:, 20]], tbl_21[ids[:, 21]], tbl_22[ids[:, 22]], tbl_23[ids[:, 23]], tbl_24[ids[:, 24]], tbl_25[ids[:, 25]], tbl_26[ids[:, 26]], tbl_27[ids[:, 27]], tbl_28[ids[:, 28]], tbl_29[ids[:, 29]], tbl_30[ids[:, 30]], tbl_31[ids[:, 31]], tbl_32[ids[:, 32]], tbl_33[ids[:, 33]], tbl_34[ids[:, 34]], tbl_35[ids[:, 35]], tbl_36[ids[:, 36]], tbl_37[ids[:, 37]], tbl_38[ids[:, 38]], tbl_39[ids[:, 39]]], axis=1)
    z = _L0_rec_ref(e, L0_rec_bilinear_matrices)
    z = z.reshape(z.shape[0], -1)
    h = jnp.concatenate([z, dense_ctx], axis=1)
    h = jnp.maximum(h @ W_top1 + b_top1, 0.0)
    h = jnp.maximum(h @ W_top2 + b_top2, 0.0)
    y = h @ W_top3
    return y

_drawn_inputs = setup_inputs


def setup_inputs(seed=0):
    import zlib

    import numpy as np

    out = dict(_drawn_inputs(seed))
    spreads = {'b_top1': (0.0, 0.1), 'b_top2': (0.0, 0.1)}
    factors = {'tbl_0': 3.545,
     'tbl_1': 3.496,
     'tbl_2': 3.452,
     'tbl_3': 2.998,
     'tbl_4': 3.186,
     'tbl_5': 3.057,
     'tbl_6': 3.445,
     'tbl_7': 3.457,
     'tbl_8': 2.914,
     'tbl_9': 3.097,
     'tbl_10': 3.108,
     'tbl_11': 3.366,
     'tbl_12': 2.848,
     'tbl_13': 3.184,
     'tbl_14': 3.05,
     'tbl_15': 3.273,
     'tbl_16': 3.224,
     'tbl_17': 3.118,
     'tbl_18': 3.545,
     'tbl_19': 3.353,
     'tbl_20': 2.893,
     'tbl_21': 3.4,
     'tbl_22': 3.086,
     'tbl_23': 3.026,
     'tbl_24': 3.35,
     'tbl_25': 3.405,
     'tbl_26': 3.024,
     'tbl_27': 3.334,
     'tbl_28': 3.02,
     'tbl_29': 3.127,
     'tbl_30': 3.025,
     'tbl_31': 2.921,
     'tbl_32': 3.287,
     'tbl_33': 3.074,
     'tbl_34': 3.175,
     'tbl_35': 3.076,
     'tbl_36': 3.409,
     'tbl_37': 3.197,
     'tbl_38': 3.402,
     'tbl_39': 3.211}
    for name, (base, spread) in spreads.items():
        noise = np.random.default_rng([zlib.crc32(name.encode()), seed]).standard_normal(out[name].shape)
        drawn = base * np.exp(spread * noise) if base else spread * noise
        out[name] = jnp.asarray(drawn.astype(out[name].dtype))
    for name, factor in factors.items():
        out[name] = (out[name] * factor).astype(out[name].dtype)
    return out
```

```python
from contextlib import ExitStack

import numpy as np

import concourse.bass as bass
from concourse import mybir

F32 = mybir.dt.float32
F32R = mybir.dt.float32r
I32 = mybir.dt.int32
ALU = mybir.AluOpType
ACT = mybir.ActivationFunctionType

P = 128
BATCH, FIELDS, DIM, DENSE = 512, 40, 32, 16
HALF = BATCH // 2
BT = HALF // P
G = P // DIM
GROUPS = FIELDS // G
SETS = 2 * GROUPS
UNITS = GROUPS * (GROUPS + 1) // 2
PER_BLOCK = DIM // G
BLOCKS = -(-UNITS // PER_BLOCK)
N1, N2 = 512, 256
M1, M2 = N1 // P, N2 // P

UNIT = [(t, u) for t in range(GROUPS) for u in range(t + 1)]


def tiles_in(v):
    t, u = UNIT[v]
    return G - 1 if t == u else G


TILE0 = [sum(tiles_in(w) for w in range(v)) for v in range(UNITS + 1)]
CHUNK_Q = [3] + [5] * 10
CHUNKS = len(CHUNK_Q)
CHUNK0 = [G * sum(CHUNK_Q[:c]) for c in range(CHUNKS + 1)]
TILES = CHUNK0[-1]
QMAX = max(CHUNK_Q)
SPLIT_BY = [3, 4, 5, 6, 7, 9, 10, CHUNKS]
XR_RING, P_RING = 4, 3
INSIDE = 5
SEL_COLS = DIM - G


def first_unit(b):
    return b * PER_BLOCK


def last_unit(b):
    return min((b + 1) * PER_BLOCK, UNITS) - 1


PIECES = 3


def stacked(n, part):
    first = G * (n % GROUPS) + 2 * part
    return range(first, min(first + 2, FIELDS - 1))


def units_before(n):
    h, t = divmod(n, GROUPS)
    return h * UNITS + t * (t + 1) // 2


def schedule():
    steps = [("set", 0), ("split", 0), ("stack0", 0), ("stack1", 0)]
    pending = []

    def sums(upto):
        while pending and pending[0] <= upto:
            U = pending.pop(0)
            steps.append(("sum", U))
            h, v = divmod(U, UNITS)
            if v == last_unit(v // PER_BLOCK):
                B = h * BLOCKS + v // PER_BLOCK
                steps.append(("z", B))
                late.append((U + 1, B))

    late = []
    for n in range(SETS):
        h, t = divmod(n, GROUPS)
        for u in range(t + 1):
            U = h * UNITS + t * (t + 1) // 2 + u
            if t >= INSIDE and 1 <= u <= 3:
                steps.append((("split", "stack0", "stack1")[u - 1], n))
            if INSIDE - 1 <= t < GROUPS - 1 and u == t:
                steps.append(("set", n + 1))
            steps.append(("mul", U))
            pending.append(U)
            sums(U - 2)
            if h == 1:
                while late and late[0][0] + 2 <= U:
                    steps.append(("l1", late.pop(0)[1]))
        if h == 1 and t < 2:
            sums(n * UNITS)
            while late and (t == 1 or late[0][1] < 4):
                steps.append(("l1", late.pop(0)[1]))
        if h == 1 and t == 2:
            steps.append(("head", 0))
        if (t < INSIDE - 1 or t == GROUPS - 1) and n + 1 < SETS:
            steps += [("set", n + 1), ("split", n + 1), ("stack0", n + 1), ("stack1", n + 1)]
    sums(2 * UNITS)
    steps += [("l1", B) for _, B in late] + [("head", 1)]
    return steps


def bass_dlrm_tower(nc, ids, tables, dense, mats, w1, b1, w2, b2, w3, ident, spread_bits, select, out):
    steps = schedule()
    with ExitStack() as ctx:
        def sb(name, shape, dt=F32):
            return ctx.enter_context(nc.sbuf_tensor(name, shape, dt))

        def ps(name, shape, dt=F32):
            return ctx.enter_context(nc.psum_tensor(name, shape, dt))

        def sem(name):
            return ctx.enter_context(nc.semaphore(name))

        ids_sb = sb("ids_sb", [P, 2 * BT, FIELDS], I32)
        x_rows = sb("x_rows", [P, XR_RING, BT, G, DIM])
        xt = sb("xt", [P, 2, HALF])
        xt_hi = sb("xt_hi", [P, 2, HALF], F32R)
        xt_lo = sb("xt_lo", [P, 2, HALF], F32R)
        x_stack = sb("x_stack", [P, FIELDS - 1, HALF], F32R)
        m_stack = sb("m_stack", [P, TILES, P], F32R)
        stage = sb("stage", [P, 3, 2, QMAX * P])
        prod = sb("prod", [P, P_RING, G, HALF])
        z_t = sb("z_t", [P, BLOCKS, HALF])
        h1 = sb("h1", [P, M1, HALF])
        h2 = sb("h2", [P, M2, HALF])
        y = sb("y", [1, BATCH])
        w2_sb = sb("w2_sb", [P, M1, N2])
        w3_sb = sb("w3_sb", [P, M2])
        b1_sb = sb("b1_sb", [P, M1])
        b2_sb = sb("b2_sb", [P, M2])
        eye = sb("eye", [P, P])
        spread = sb("spread", [P, G, 6 * DIM], F32R)
        sel = sb("sel", [P, SEL_COLS + DIM])
        dense_pad = sb("dense_pad", [P, 2 * BT, G, DIM])
        w1_sb = stage[:].rearrange("p a b c -> p (a b c)")[:, 0:BLOCKS * N1].rearrange("p (b n) -> p b n", b=BLOCKS)

        spread_raw = prod[:, 0, :, 0:6 * DIM]

        y_ps = ps("y_ps", [P, 2, G, HALF])
        z_ps = ps("z_ps", [P, 512])
        t_ps = ps("t_ps", [P, 2, HALF])
        h_ps = ps("h_ps", [P, M1, HALF])

        ids_in = sem("ids_in")
        eye_in = sem("eye_in")
        consts_in = sem("consts_in")
        pad_zeroed = sem("pad_zeroed")
        dense_in = sem("dense_in")
        w1_in = sem("w1_in")
        spread_in = sem("spread_in")
        spread_done = sem("spread_done")
        gathered = [sem(f"gathered{k}") for k in range(XR_RING)]
        raw_in = [sem(f"raw_in{k}") for k in range(2)]
        m_hi_done = sem("m_hi_done")
        m_lo_done = sem("m_lo_done")
        m_in_stack = [sem(f"m_in_stack{c}") for c in range(CHUNKS)]
        xt_done = sem("xt_done")
        xt_lo_done = sem("xt_lo_done")
        piece_done = sem("piece_done")
        piece_out = sem("piece_out")
        y_done = sem("y_done")
        prod_done = sem("prod_done")
        sum_done = sem("sum_done")
        z_out = sem("z_out")
        l1_done = sem("l1_done")
        h1_done = sem("h1_done")
        l1_out = sem("l1_out")
        l2_done = sem("l2_done")
        l2_out = sem("l2_out")
        l3_done = sem("l3_done")
        y_out = sem("y_out")
        stored = sem("stored")
        block = ctx.enter_context(nc.Block())

        def stage_slot(kind, c, dt=F32):
            s = stage[:, kind, c % 2, 0:CHUNK_Q[c] * P]
            return s if dt == F32 else s.bitcast(dt)

        @block.gpsimd
        def _(pool):
            pool.wait_ge(ids_in, 16)
            for n in range(SETS):
                h, t = divmod(n, GROUPS)
                if n >= XR_RING:
                    pool.wait_ge(piece_done, PIECES * (n - XR_RING) + 1)
                for bt in range(BT):
                    for f in range(G):
                        row = bass.IndirectOffsetOnAxis(ap=ids_sb[:, BT * h + bt, G * t + f:G * t + f + 1], axis=0)
                        pool.indirect_dma_start(out=x_rows[:, n % XR_RING, bt, f, :], out_offset=None,
                                                in_=tables[G * t + f], in_offset=row
                                                ).then_inc(gathered[n % XR_RING], 16)

        @block.sync
        def _(sp):
            def load_raw(c):
                q0 = CHUNK0[c] // G
                sp.dma_start(stage_slot(0, c), mats[:, q0 * P:(q0 + CHUNK_Q[c]) * P]).then_inc(raw_in[c % 2], 16)

            sp.dma_start(ids_sb[:], ids).then_inc(ids_in, 16)
            load_raw(0)
            load_raw(1)
            for c in range(CHUNKS):
                sp.wait_ge(m_hi_done, c + 1)
                sp.wait_ge(m_lo_done, c + 1)
                if c + 2 < CHUNKS:
                    load_raw(c + 2)
                q = CHUNK_Q[c]
                for g in range(G):
                    tile0 = CHUNK0[c] + g * q
                    for row in range(4):
                        src = stage_slot(1 + row % 2, c)[g * DIM:(g + 1) * DIM, :]
                        dst = m_stack[row * DIM:(row + 1) * DIM, tile0:tile0 + q, :]
                        sp.dma_start(dst.rearrange("p q c -> p (q c)").bitcast(F32), src).then_inc(m_in_stack[c], 16)
            for c in range(CHUNKS):
                sp.wait_ge(m_in_stack[c], 16 * 4 * G)
            sp.dma_start(w1_sb, w1).then_inc(w1_in, 16)
            sp.wait_ge(y_out, 2)
            sp.dma_start(out.rearrange("b o -> o b"), y[:]).then_inc(stored, 16)
            sp.wait_ge(stored, 16)

        @block.scalar
        def _(act):
            act.dma_start(eye[:], ident).then_inc(eye_in, 16)
            act.dma_start(spread_raw, spread_bits).then_inc(spread_in, 16)
            act.dma_start(sel[:], select).then_inc(consts_in, 16)
            act.dma_start(w2_sb[:], w2).then_inc(consts_in, 16)
            act.dma_start(w3_sb[:], w3).then_inc(consts_in, 16)
            act.dma_start(b1_sb[:], b1).then_inc(consts_in, 16)
            act.dma_start(b2_sb[:], b2).then_inc(consts_in, 16)
            act.wait_ge(pad_zeroed, 1)
            for bt in range(2 * BT):
                act.dma_start(dense_pad[:, bt, :, DIM - G:DIM], dense[bt * P:(bt + 1) * P, :].rearrange(
                    "p (s q) -> p s q", s=G)).then_inc(dense_in, 16)
            split = 0
            consts_seen = False
            for what, k in steps:
                if what == "set":
                    n = k
                    while n < GROUPS and split < SPLIT_BY[min(n, len(SPLIT_BY) - 1)]:
                        c = split
                        act.wait_ge(raw_in[c % 2], 16 * (c // 2 + 1))
                        if c >= 2:
                            act.wait_ge(m_in_stack[c - 2], 16 * 4 * G)
                        nc.scalar.activation(stage_slot(1, c, F32R), stage_slot(0, c), ACT.Copy).then_inc(m_hi_done, 1)
                        split += 1
                    act.wait_ge(piece_done, PIECES * n + 1)
                    if n >= 2:
                        act.wait_ge(prod_done, units_before(n - 1))
                    nc.scalar.activation(xt[:, n % 2, :], t_ps[:, 0, :], ACT.Copy).then_inc(xt_done, 1)
                    nc.scalar.activation(xt_hi[:, n % 2, :], t_ps[:, 0, :], ACT.Copy).then_inc(piece_out, 1)
                if what in ("stack0", "stack1"):
                    n, part = k, int(what[-1])
                    h, t = divmod(n, GROUPS)
                    act.wait_ge(piece_done, PIECES * n + part + 2)
                    if h == 1:
                        act.wait_ge(y_done, UNITS - GROUPS + t + 1)
                    fields = stacked(n, part)
                    nc.scalar.activation(x_stack[:, fields[0]:fields[-1] + 1, :], t_ps[:, 0:len(fields), :],
                                         ACT.Copy).then_inc(piece_out, 1)
                if what == "z":
                    h, b = divmod(k, BLOCKS)
                    act.wait_ge(sum_done, h * UNITS + last_unit(b) + 1)
                    if h == 1:
                        act.wait_ge(l1_done, b + 1)
                    nc.scalar.activation(z_t[:, b, :], z_ps[:, 0:HALF], ACT.Copy).then_inc(z_out, 1)
                if what == "head":
                    if not consts_seen:
                        act.wait_ge(consts_in, 16 * 5)
                        consts_seen = True
                    if k == 1:
                        act.wait_ge(l2_done, 1)
                    for m in range(M1):
                        act.wait_ge(h1_done, M1 * k + 2 * (m // 2) + 2)
                        nc.scalar.activation(h1[:, m, :], h_ps[:, m, :], ACT.Relu,
                                             bias=b1_sb[:, m:m + 1]).then_inc(l1_out, 1)
                    if k == 1:
                        act.wait_ge(l3_done, 1)
                    act.wait_ge(l2_done, k + 1)
                    for m in range(M2):
                        nc.scalar.activation(h2[:, m, :], h_ps[:, m, :], ACT.Relu,
                                             bias=b2_sb[:, m:m + 1]).then_inc(l2_out, 1)
                    act.wait_ge(l3_done, k + 1)
                    nc.scalar.activation(y[:, k * HALF:(k + 1) * HALF], h_ps[0:1, M2, :], ACT.Copy).then_inc(y_out, 1)

        @block.vector
        def _(dve):
            nc.vector.memset(dense_pad[:], 0.0).then_inc(pad_zeroed, 1)
            dve.wait_ge(spread_in, 16)
            nc.vector.tensor_copy(spread[:], spread_raw).then_inc(spread_done, 1)
            split = 0
            for what, k in steps:
                if what == "set":
                    n = k
                    while n < GROUPS and split < SPLIT_BY[min(n, len(SPLIT_BY) - 1)]:
                        c = split
                        dve.wait_ge(m_hi_done, c + 1)
                        if c >= 2:
                            dve.wait_ge(m_in_stack[c - 2], 16 * 4 * G)
                        nc.vector.tensor_tensor(stage_slot(2, c, F32R), stage_slot(0, c), stage_slot(1, c),
                                                ALU.subtract).then_inc(m_lo_done, 1)
                        split += 1
                if what == "split":
                    n = k
                    dve.wait_ge(xt_done, n + 1)
                    dve.wait_ge(piece_out, PIECES * n + 1)
                    if n >= 2:
                        dve.wait_ge(piece_done, PIECES * (n - 1))
                    nc.vector.tensor_tensor(xt_lo[:, n % 2, :], xt[:, n % 2, :], xt_hi[:, n % 2, :].bitcast(F32),
                                            ALU.subtract).then_inc(xt_lo_done, 1)
                if what == "mul":
                    h, v = divmod(k, UNITS)
                    t, u = UNIT[v]
                    n = h * GROUPS + t
                    w = tiles_in(v)
                    if u == 0:
                        dve.wait_ge(xt_done, n + 1)
                    dve.wait_ge(y_done, k + 1)
                    if k >= P_RING:
                        dve.wait_ge(sum_done, k - P_RING + 1)
                    nc.vector.tensor_tensor(prod[:, k % P_RING, 0:w, :], y_ps[:, k % 2, 0:w, :],
                                            xt[:, n % 2, :].unsqueeze(1).to_broadcast([P, w, HALF]),
                                            ALU.mult).then_inc(prod_done, 1)

        @block.tensor
        def _(pe):
            pe.wait_ge(eye_in, 16)
            chunks_seen = 0
            for what, k in steps:
                if what == "set":
                    n = k
                    pe.wait_ge(gathered[n % XR_RING], 16 * BT * G * (n // XR_RING + 1))
                    if n >= 1:
                        pe.wait_ge(piece_out, PIECES * n)
                    for bt in range(BT):
                        rows = x_rows[:, n % XR_RING, bt, :, :].rearrange("p f d -> p (f d)")
                        last = nc.tensor.transpose(t_ps[:, 0, bt * P:(bt + 1) * P], rows, eye[:])
                    last.then_inc(piece_done, 1)
                if what in ("stack0", "stack1"):
                    n, part = k, int(what[-1])
                    if k == 0 and part == 0:
                        pe.wait_ge(spread_done, 1)
                    pe.wait_ge(xt_lo_done, n + 1)
                    pe.wait_ge(piece_out, PIECES * n + part + 1)
                    for slot, field in enumerate(stacked(n, part)):
                        f = field % G
                        nc.tensor.matmul(t_ps[:, slot, :], spread[:, f, 2 * DIM:6 * DIM], xt_hi[:, n % 2, :],
                                         start=True, stop=False)
                        last = nc.tensor.matmul(t_ps[:, slot, :], spread[:, f, 0:4 * DIM], xt_lo[:, n % 2, :],
                                                start=False, stop=True)
                    last.then_inc(piece_done, 1)
                if what == "mul":
                    h, v = divmod(k, UNITS)
                    t, u = UNIT[v]
                    n = h * GROUPS + t
                    while CHUNK0[chunks_seen] < TILE0[v + 1] and chunks_seen < CHUNKS and h == 0:
                        pe.wait_ge(m_in_stack[chunks_seen], 16 * 4 * G)
                        chunks_seen += 1
                    if u == t:
                        pe.wait_ge(piece_out, PIECES * (n + 1))
                    if k >= 2:
                        pe.wait_ge(prod_done, k - 1)
                    for s in range(tiles_in(v)):
                        last = nc.tensor.matmul(y_ps[:, k % 2, s, :], m_stack[:, TILE0[v] + s, :],
                                                x_stack[:, G * u + s, :], start=True, stop=True)
                    last.then_inc(y_done, 1)
                if what == "sum":
                    h, v = divmod(k, UNITS)
                    b, r = divmod(v, PER_BLOCK)
                    B = h * BLOCKS + b
                    if k == 0:
                        pe.wait_ge(consts_in, 16 * 5)
                    if r == 0 and B >= 1:
                        pe.wait_ge(z_out, B)
                    started = [first_unit(b) + (tiles_in(first_unit(b)) <= s) for s in range(G)]
                    if b == BLOCKS - 1 and r == 0:
                        pe.wait_ge(dense_in, 16 * 2 * BT)
                        for s in range(G):
                            for bt in range(BT):
                                nc.tensor.matmul(z_ps[s * DIM:(s + 1) * DIM, bt * P:(bt + 1) * P],
                                                 dense_pad[:, BT * h + bt, s, :], eye[:], start=(bt == 0),
                                                 stop=False, skip_group_check=True)
                        started = [-1] * G
                    pe.wait_ge(prod_done, k + 1)
                    for s in range(tiles_in(v)):
                        window = sel[:, SEL_COLS - G * r:SEL_COLS - G * r + DIM]
                        last = nc.tensor.matmul(z_ps[s * DIM:(s + 1) * DIM, 0:HALF], window,
                                                prod[:, k % P_RING, s, :], start=(v == started[s]),
                                                stop=(v >= last_unit(b) - 1), skip_group_check=True)
                    last.then_inc(sum_done, 1)
                if what == "l1":
                    h, b = divmod(k, BLOCKS)
                    pe.wait_ge(z_out, k + 1)
                    if k == 0:
                        pe.wait_ge(w1_in, 16)
                    if k == BLOCKS:
                        pe.wait_ge(y_out, 1)
                    for m in range(M1):
                        last = nc.tensor.matmul(h_ps[:, m, :], w1_sb[:, b, m * P:(m + 1) * P], z_t[:, b, :],
                                                start=(b == 0 and m % 2 == 0), stop=(b == BLOCKS - 1),
                                                skip_group_check=True)
                        if b == BLOCKS - 1:
                            last.then_inc(h1_done, 1)
                    if b < BLOCKS - 1:
                        last.then_inc(l1_done, 1)
                if what == "head":
                    for m in range(M1):
                        pe.wait_ge(l1_out, M1 * k + max(m + 1, M2))
                        for c in range(M2):
                            last = nc.tensor.matmul(h_ps[:, c, :], w2_sb[:, m, c * P:(c + 1) * P], h1[:, m, :],
                                                    start=(m == 0 and c == 0), stop=(m == M1 - 1),
                                                    skip_group_check=True)
                    last.then_inc(l2_done, 1)
                    for c in range(M2):
                        pe.wait_ge(l2_out, M2 * k + c + 1)
                        last = nc.tensor.matmul(h_ps[0:1, M2, :], w3_sb[:, c:c + 1], h2[:, c, :],
                                                start=(c == 0), stop=(c == M2 - 1), skip_group_check=True)
                    last.then_inc(l3_done, 1)


def pair_index(i, j):
    return i * FIELDS - i * (i + 1) // 2 + j - i - 1


def kernel(**inputs):
    import concourse.bacc as bacc
    from concourse.bass_utils import run_bass_kernel_spmd

    a = {k: np.asarray(v) for k, v in inputs.items()}
    pairs = a["L0_rec_bilinear_matrices"]
    tiles = np.zeros((TILES, DIM, G, DIM), pairs.dtype)
    w_top1 = a["W_top1"]
    w1 = np.zeros((BLOCKS, P, N1), w_top1.dtype)
    for v, (t, u) in enumerate(UNIT):
        b, r = divmod(v, PER_BLOCK)
        for s in range(tiles_in(v)):
            for jj in range(G):
                i, j = G * u + s, G * t + jj
                if i < j:
                    tiles[TILE0[v] + s, :, jj, :] = pairs[pair_index(i, j)]
                    w1[b, DIM * s + G * r + jj] = w_top1[pair_index(i, j)]
    for q in range(DENSE):
        w1[BLOCKS - 1, DIM * (q // G) + DIM - G + q % G] = w_top1[FIELDS * (FIELDS - 1) // 2 + q]
    tiles = tiles.reshape(TILES, DIM, P)
    mats = np.concatenate([
        tiles[CHUNK0[c]:CHUNK0[c + 1]].reshape(G, CHUNK_Q[c], DIM, P).transpose(0, 2, 1, 3).reshape(P, CHUNK_Q[c] * P)
        for c in range(CHUNKS)], axis=1)
    select = np.zeros((P, SEL_COLS + DIM), np.float32)
    for p in range(P):
        select[p, SEL_COLS + p // DIM] = 1.0
    spread = np.zeros((P, G, 6, DIM), np.float32)
    for p in range(P):
        spread[p, p // DIM, 2:4, p % DIM] = 1.0
    arrays = {
        "ids": a["ids"].reshape(2 * BT, P, FIELDS).transpose(1, 0, 2),
        "dense": a["dense_ctx"],
        "mats": mats,
        "w1": w1.transpose(1, 0, 2),
        "b1": a["b_top1"].reshape(M1, P).T,
        "w2": a["W_top2"].reshape(M1, P, N2).transpose(1, 0, 2),
        "b2": a["b_top2"].reshape(M2, P).T,
        "w3": a["W_top3"].reshape(M2, P).T,
        "ident": np.eye(P, dtype=np.float32),
        "spread_bits": spread.reshape(P, G, 6 * DIM),
        "select": select,
    }
    arrays |= {f"tbl_{f}": a[f"tbl_{f}"] for f in range(FIELDS)}
    arrays = {k: np.ascontiguousarray(v) for k, v in arrays.items()}

    nc = bacc.Bacc("TRN2", target_bir_lowering=False, num_devices=1)
    dram = {k: nc.dram_tensor(k, v.shape, mybir.dt.from_np(v.dtype), kind="ExternalInput").ap() for k, v in arrays.items()}
    out = nc.dram_tensor("out", (BATCH, 1), F32, kind="ExternalOutput").ap()
    tables = [dram.pop(f"tbl_{f}") for f in range(FIELDS)]
    bass_dlrm_tower(nc, tables=tables, out=out, **dram)
    r = run_bass_kernel_spmd(nc, [arrays], core_ids=[0])
    return r.results[0]["out"]
```

```python
from contextlib import ExitStack

import numpy as np

import concourse.bass as bass
from concourse import mybir

F32 = mybir.dt.float32
F32R = mybir.dt.float32r
I32 = mybir.dt.int32
ALU = mybir.AluOpType
ACT = mybir.ActivationFunctionType

P = 128
BATCH, FIELDS, DIM, DENSE = 512, 40, 32, 16
HALF = BATCH // 2
BT = HALF // P
G = P // DIM
GROUPS = FIELDS // G
SETS = 2 * GROUPS
UNITS = GROUPS * (GROUPS + 1) // 2
PER_BLOCK = DIM // G
BLOCKS = -(-UNITS // PER_BLOCK)
N1, N2 = 512, 256
M1, M2 = N1 // P, N2 // P

UNIT = [(t, u) for t in range(GROUPS) for u in range(t + 1)]


def tiles_in(v):
    t, u = UNIT[v]
    return G - 1 if t == u else G


TILE0 = [sum(tiles_in(w) for w in range(v)) for v in range(UNITS + 1)]
CHUNK_Q = [5] + [8] * 6
CHUNKS = len(CHUNK_Q)
CHUNK0 = [G * sum(CHUNK_Q[:c]) for c in range(CHUNKS + 1)]
TILES = CHUNK0[-1]
QMAX = max(CHUNK_Q)
CHUNK_AFTER = {(1, 1): 2, (2, 2): 3, (3, 3): 4, (5, 2): 5, (6, 3): 6}
XR_RING, P_RING = 6, 3
EAGER = (7, 1)
SEL_COLS = DIM - G


def first_unit(b):
    return b * PER_BLOCK


def last_unit(b):
    return min((b + 1) * PER_BLOCK, UNITS) - 1


PIECES = 3


def stacked(n, part):
    first = G * (n % GROUPS) + 2 * part
    return range(first, min(first + 2, FIELDS - 1))


def units_before(n):
    h, t = divmod(n, GROUPS)
    return h * UNITS + t * (t + 1) // 2


def schedule():
    steps = [("chunk", 0), ("chunk", 1), ("set", 0), ("split", 0), ("stack0", 0), ("stack1", 0)]
    unsummed, mlp = [], []

    def sums(upto):
        while unsummed and unsummed[0] <= upto:
            U = unsummed.pop(0)
            steps.append(("sum", U))
            h, v = divmod(U, UNITS)
            if v == last_unit(v // PER_BLOCK):
                B = h * BLOCKS + v // PER_BLOCK
                steps.append(("z", B))
                mlp.append(("l1", B))
                if v == UNITS - 1:
                    mlp.extend([("l2", h), ("l3", h)])

    def mlp_step(h):
        if h == 1 and mlp:
            steps.append(mlp.pop(0))

    for n in range(SETS):
        h, t = divmod(n, GROUPS)
        for u in range(t + 1):
            U = h * UNITS + t * (t + 1) // 2 + u
            if n > 0 and (u in (1, 2, 3) if t >= 3 else u == min(t, 1)) and n != GROUPS:
                for what in (("split", "stack0", "stack1")[u - 1],) if t >= 3 else ("split", "stack0", "stack1"):
                    steps.append((what, n))
                    mlp_step(h)
            if u == t and t + 1 in range(EAGER[h], GROUPS):
                steps.append(("set", n + 1))
                mlp_step(h)
            if n == GROUPS - 1 and u > GROUPS - 4:
                steps.append((("set", "split", "stack0")[u - GROUPS + 3], n + 1))
            steps.append(("mul", U))
            unsummed.append(U)
            sums(U - 2)
            if (n, u) in CHUNK_AFTER:
                steps.append(("chunk", CHUNK_AFTER[n, u]))
            if t >= 5 and u % 2:
                mlp_step(h)
        if n == GROUPS - 1:
            steps.append(("stack1", n + 1))
        elif t + 1 < EAGER[h]:
            steps.append(("set", n + 1))
    sums(2 * UNITS)
    return steps + mlp


def bass_dlrm_tower(nc, ids, tables, dense, mats, w1, b1, w2, b2, w3, ident, spread_bits, select, out):
    steps = schedule()
    with ExitStack() as ctx:
        def sb(name, shape, dt=F32):
            return ctx.enter_context(nc.sbuf_tensor(name, shape, dt))

        def ps(name, shape, dt=F32):
            return ctx.enter_context(nc.psum_tensor(name, shape, dt))

        def sem(name):
            return ctx.enter_context(nc.semaphore(name))

        ids_sb = sb("ids_sb", [P, 2 * BT, FIELDS], I32)
        x_rows = sb("x_rows", [P, XR_RING, BT, G, DIM])
        xt = sb("xt", [P, 2, HALF])
        xt_hi = sb("xt_hi", [P, 2, HALF], F32R)
        xt_lo = sb("xt_lo", [P, 2, HALF], F32R)
        x_stack = sb("x_stack", [P, FIELDS - 1, HALF], F32R)
        m_stack = sb("m_stack", [P, TILE0[UNITS], P], F32R)
        stage = sb("stage", [P, 2, 2, QMAX * P])
        prod = sb("prod", [P, P_RING, G, HALF])
        z_t = sb("z_t", [P, BLOCKS, HALF])
        h1 = sb("h1", [P, M1, HALF])
        y = sb("y", [1, BATCH])
        w2_sb = sb("w2_sb", [P, M1, N2])
        w3_sb = sb("w3_sb", [P, M2])
        b1_sb = sb("b1_sb", [P, M1])
        b2_sb = sb("b2_sb", [P, M2])
        eye = sb("eye", [P, P])
        spread = sb("spread", [P, G, 6 * DIM], F32R)
        sel = sb("sel", [P, SEL_COLS + DIM])
        dense_pad = sb("dense_pad", [P, 2 * BT, G, DIM])
        stage_flat = stage[:].rearrange("p a b c -> p (a b c)")
        h2 = stage_flat[:, BLOCKS * N1:BLOCKS * N1 + M2 * HALF].rearrange("p (c b) -> p c b", c=M2)
        w1_sb = stage_flat[:, 0:BLOCKS * N1].rearrange("p (b n) -> p b n", b=BLOCKS)

        spread_raw = prod[:, 0, :, 0:6 * DIM]

        y_ps = ps("y_ps", [P, 2, G, HALF])
        z_ps = ps("z_ps", [P, 512])
        t_ps = ps("t_ps", [P, 2, HALF])
        h_ps = ps("h_ps", [P, M1, HALF])

        ids_in = sem("ids_in")
        eye_in = sem("eye_in")
        sel_in = sem("sel_in")
        head_in = sem("head_in")
        pad_zeroed = sem("pad_zeroed")
        dense_in = sem("dense_in")
        w1_in = sem("w1_in")
        spread_in = sem("spread_in")
        spread_done = sem("spread_done")
        gathered = [sem(f"gathered{k}") for k in range(XR_RING)]
        raw_in = [sem(f"raw_in{k}") for k in range(2)]
        m_hi_done = sem("m_hi_done")
        m_lo_done = sem("m_lo_done")
        m_in_stack = [sem(f"m_in_stack{c}") for c in range(CHUNKS)]
        xt_done = sem("xt_done")
        xt_lo_done = sem("xt_lo_done")
        piece_done = sem("piece_done")
        piece_out = sem("piece_out")
        y_done = sem("y_done")
        prod_done = sem("prod_done")
        sum_done = sem("sum_done")
        z_out = sem("z_out")
        l1_done = sem("l1_done")
        h1_done = sem("h1_done")
        l1_out = sem("l1_out")
        l2_done = sem("l2_done")
        l2_out = sem("l2_out")
        l3_done = sem("l3_done")
        y_out = sem("y_out")
        stored = sem("stored")
        block = ctx.enter_context(nc.Block())

        def stage_slot(kind, c, dt=F32):
            s = stage[:, kind, c % 2, 0:CHUNK_Q[c] * P]
            return s if dt == F32 else s.bitcast(dt)

        @block.gpsimd
        def _(pool):
            pool.wait_ge(ids_in, 16)
            for n in range(SETS):
                h, t = divmod(n, GROUPS)
                if n >= XR_RING:
                    pool.wait_ge(piece_done, PIECES * (n - XR_RING) + 1)
                for bt in range(BT):
                    for f in range(G):
                        row = bass.IndirectOffsetOnAxis(ap=ids_sb[:, BT * h + bt, G * t + f:G * t + f + 1], axis=0)
                        pool.indirect_dma_start(out=x_rows[:, n % XR_RING, bt, f, :], out_offset=None,
                                                in_=tables[G * t + f], in_offset=row
                                                ).then_inc(gathered[n % XR_RING], 16)

        @block.sync
        def _(sp):
            def load_raw(c):
                q0 = CHUNK0[c] // G
                sp.dma_start(stage_slot(0, c), mats[:, q0 * P:(q0 + CHUNK_Q[c]) * P]).then_inc(raw_in[c % 2], 16)

            sp.dma_start(ids_sb[:], ids).then_inc(ids_in, 16)
            load_raw(0)
            load_raw(1)
            sp.wait_ge(pad_zeroed, 1)
            for c in range(CHUNKS):
                sp.wait_ge(m_hi_done, c + 1)
                sp.wait_ge(m_lo_done, c + 1)
                q = CHUNK_Q[c]
                for g in range(G):
                    if g == 1 and 1 <= c < CHUNKS - 1:
                        sp.wait_ge(m_in_stack[c - 1], 16 * 4 * G)
                        load_raw(c + 1)
                    tile0 = CHUNK0[c] + g * q
                    w = min(q, TILE0[UNITS] - tile0)
                    for row in range(4):
                        src = stage_slot(1 - row % 2, c)[g * DIM:(g + 1) * DIM, 0:w * P]
                        dst = m_stack[row * DIM:(row + 1) * DIM, tile0:tile0 + w, :]
                        sp.dma_start(dst.rearrange("p q c -> p (q c)").bitcast(F32), src).then_inc(m_in_stack[c], 16)
            for bt in range(2 * BT):
                sp.dma_start(dense_pad[:, bt, :, DIM - G:DIM], dense[bt * P:(bt + 1) * P, :].rearrange(
                    "p (s q) -> p s q", s=G)).then_inc(dense_in, 16)
            for c in range(CHUNKS):
                sp.wait_ge(m_in_stack[c], 16 * 4 * G)
            sp.dma_start(w1_sb, w1).then_inc(w1_in, 16)
            sp.dma_start(w2_sb[:], w2).then_inc(head_in, 16)
            sp.dma_start(w3_sb[:], w3).then_inc(head_in, 16)
            sp.dma_start(b1_sb[:], b1).then_inc(head_in, 16)
            sp.dma_start(b2_sb[:], b2).then_inc(head_in, 16)
            sp.wait_ge(y_out, 2)
            sp.dma_start(out.rearrange("b o -> o b"), y[:]).then_inc(stored, 16)
            sp.wait_ge(stored, 16)

        @block.scalar
        def _(act):
            act.dma_start(eye[:], ident).then_inc(eye_in, 16)
            act.dma_start(spread_raw, spread_bits).then_inc(spread_in, 16)
            act.dma_start(sel[:], select).then_inc(sel_in, 16)
            for what, k in steps:
                if what == "chunk":
                    c = k
                    act.wait_ge(raw_in[c % 2], 16 * (c // 2 + 1))
                    if c >= 2:
                        act.wait_ge(m_in_stack[c - 2], 16 * 4 * G)
                    nc.scalar.activation(stage_slot(1, c, F32R), stage_slot(0, c), ACT.Copy).then_inc(m_hi_done, 1)
                if what == "set":
                    n = k
                    act.wait_ge(piece_done, PIECES * n + 1)
                    if n >= 2:
                        act.wait_ge(prod_done, units_before(n - 1))
                    nc.scalar.activation(xt[:, n % 2, :], t_ps[:, 0, :], ACT.Copy).then_inc(xt_done, 1)
                    nc.scalar.activation(xt_hi[:, n % 2, :], t_ps[:, 0, :], ACT.Copy).then_inc(piece_out, 1)
                if what in ("stack0", "stack1"):
                    n, part = k, int(what[-1])
                    h, t = divmod(n, GROUPS)
                    act.wait_ge(piece_done, PIECES * n + part + 2)
                    if h == 1:
                        act.wait_ge(y_done, UNITS - GROUPS + t + 1)
                    fields = stacked(n, part)
                    nc.scalar.activation(x_stack[:, fields[0]:fields[-1] + 1, :], t_ps[:, 0:len(fields), :],
                                         ACT.Copy).then_inc(piece_out, 1)
                if what == "z":
                    h, b = divmod(k, BLOCKS)
                    act.wait_ge(sum_done, h * UNITS + last_unit(b) + 1)
                    if h == 1:
                        act.wait_ge(l1_done, b + 1)
                    nc.scalar.activation(z_t[:, b, :], z_ps[:, 0:HALF], ACT.Copy).then_inc(z_out, 1)
                if what == "l1" and k % BLOCKS == BLOCKS - 1:
                    h = k // BLOCKS
                    act.wait_ge(head_in, 16 * 4)
                    if h == 1:
                        act.wait_ge(l2_done, 1)
                    for m in range(M1):
                        act.wait_ge(h1_done, M1 * h + 2 * (m // 2) + 2)
                        nc.scalar.activation(h1[:, m, :], h_ps[:, m, :], ACT.Relu,
                                             bias=b1_sb[:, m:m + 1]).then_inc(l1_out, 1)
                if what == "l2":
                    if k == 1:
                        act.wait_ge(l3_done, 1)
                    act.wait_ge(l2_done, k + 1)
                    for m in range(M2):
                        nc.scalar.activation(h2[:, m, :], h_ps[:, m, :], ACT.Relu,
                                             bias=b2_sb[:, m:m + 1]).then_inc(l2_out, 1)
                if what == "l3":
                    act.wait_ge(l3_done, k + 1)
                    nc.scalar.activation(y[:, k * HALF:(k + 1) * HALF], h_ps[0:1, M2, :], ACT.Copy).then_inc(y_out, 1)

        @block.vector
        def _(dve):
            nc.vector.memset(dense_pad[:], 0.0).then_inc(pad_zeroed, 1)
            dve.wait_ge(spread_in, 16)
            nc.vector.tensor_copy(spread[:], spread_raw).then_inc(spread_done, 1)
            for what, k in steps:
                if what == "chunk":
                    dve.wait_ge(m_hi_done, k + 1)
                    nc.vector.tensor_tensor(stage_slot(0, k, F32R), stage_slot(0, k), stage_slot(1, k),
                                            ALU.subtract).then_inc(m_lo_done, 1)
                if what == "split":
                    n = k
                    dve.wait_ge(xt_done, n + 1)
                    dve.wait_ge(piece_out, PIECES * n + 1)
                    if n >= 2:
                        dve.wait_ge(piece_done, PIECES * (n - 1))
                    nc.vector.tensor_tensor(xt_lo[:, n % 2, :], xt[:, n % 2, :], xt_hi[:, n % 2, :].bitcast(F32),
                                            ALU.subtract).then_inc(xt_lo_done, 1)
                if what == "mul":
                    h, v = divmod(k, UNITS)
                    t, u = UNIT[v]
                    n = h * GROUPS + t
                    w = tiles_in(v)
                    if u == 0:
                        dve.wait_ge(xt_done, n + 1)
                    dve.wait_ge(y_done, k + 1)
                    if k >= P_RING:
                        dve.wait_ge(sum_done, k - P_RING + 1)
                    nc.vector.tensor_tensor(prod[:, k % P_RING, 0:w, :], y_ps[:, k % 2, 0:w, :],
                                            xt[:, n % 2, :].unsqueeze(1).to_broadcast([P, w, HALF]),
                                            ALU.mult).then_inc(prod_done, 1)

        @block.tensor
        def _(pe):
            pe.wait_ge(eye_in, 16)
            chunks_seen = 0
            for what, k in steps:
                if what == "set":
                    n = k
                    pe.wait_ge(gathered[n % XR_RING], 16 * BT * G * (n // XR_RING + 1))
                    if n >= 1:
                        pe.wait_ge(piece_out, PIECES * n)
                    for bt in range(BT):
                        rows = x_rows[:, n % XR_RING, bt, :, :].rearrange("p f d -> p (f d)")
                        last = nc.tensor.transpose(t_ps[:, 0, bt * P:(bt + 1) * P], rows, eye[:])
                    last.then_inc(piece_done, 1)
                if what in ("stack0", "stack1"):
                    n, part = k, int(what[-1])
                    if k == 0 and part == 0:
                        pe.wait_ge(spread_done, 1)
                    pe.wait_ge(xt_lo_done, n + 1)
                    pe.wait_ge(piece_out, PIECES * n + part + 1)
                    for slot, field in enumerate(stacked(n, part)):
                        f = field % G
                        nc.tensor.matmul(t_ps[:, slot, :], spread[:, f, 2 * DIM:6 * DIM], xt_hi[:, n % 2, :],
                                         start=True, stop=False)
                        last = nc.tensor.matmul(t_ps[:, slot, :], spread[:, f, 0:4 * DIM], xt_lo[:, n % 2, :],
                                                start=False, stop=True)
                    last.then_inc(piece_done, 1)
                if what == "mul":
                    h, v = divmod(k, UNITS)
                    t, u = UNIT[v]
                    n = h * GROUPS + t
                    while CHUNK0[chunks_seen] < TILE0[v + 1] and chunks_seen < CHUNKS and h == 0:
                        pe.wait_ge(m_in_stack[chunks_seen], 16 * 4 * G)
                        chunks_seen += 1
                    if u == t:
                        pe.wait_ge(piece_out, PIECES * (n + 1))
                    if k >= 2:
                        pe.wait_ge(prod_done, k - 1)
                    for s in range(tiles_in(v)):
                        last = nc.tensor.matmul(y_ps[:, k % 2, s, :], m_stack[:, TILE0[v] + s, :],
                                                x_stack[:, G * u + s, :], start=True, stop=True)
                    last.then_inc(y_done, 1)
                if what == "sum":
                    h, v = divmod(k, UNITS)
                    b, r = divmod(v, PER_BLOCK)
                    B = h * BLOCKS + b
                    if k == 0:
                        pe.wait_ge(sel_in, 16)
                    if r == 0 and B >= 1:
                        pe.wait_ge(z_out, B)
                    started = [first_unit(b) + (tiles_in(first_unit(b)) <= s) for s in range(G)]
                    if b == BLOCKS - 1 and r == 0:
                        pe.wait_ge(dense_in, 16 * 2 * BT)
                        for s in range(G):
                            for bt in range(BT):
                                nc.tensor.matmul(z_ps[s * DIM:(s + 1) * DIM, bt * P:(bt + 1) * P],
                                                 dense_pad[:, BT * h + bt, s, :], eye[:], start=(bt == 0),
                                                 stop=False, skip_group_check=True)
                        started = [-1] * G
                    pe.wait_ge(prod_done, k + 1)
                    for s in range(tiles_in(v)):
                        window = sel[:, SEL_COLS - G * r:SEL_COLS - G * r + DIM]
                        last = nc.tensor.matmul(z_ps[s * DIM:(s + 1) * DIM, 0:HALF], window,
                                                prod[:, k % P_RING, s, :], start=(v == started[s]),
                                                stop=(v >= last_unit(b) - 1), skip_group_check=True)
                    last.then_inc(sum_done, 1)
                if what == "l1":
                    h, b = divmod(k, BLOCKS)
                    pe.wait_ge(z_out, k + 1)
                    if k == 0:
                        pe.wait_ge(w1_in, 16)
                    if k == BLOCKS:
                        pe.wait_ge(y_out, 1)
                    for m in range(M1):
                        last = nc.tensor.matmul(h_ps[:, m, :], w1_sb[:, b, m * P:(m + 1) * P], z_t[:, b, :],
                                                start=(b == 0 and m % 2 == 0), stop=(b == BLOCKS - 1),
                                                skip_group_check=True)
                        if b == BLOCKS - 1:
                            last.then_inc(h1_done, 1)
                    if b < BLOCKS - 1:
                        last.then_inc(l1_done, 1)
                if what == "l2":
                    pe.wait_ge(head_in, 16 * 4)
                    for m in range(M1):
                        pe.wait_ge(l1_out, M1 * k + max(m + 1, M2))
                        for c in range(M2):
                            last = nc.tensor.matmul(h_ps[:, c, :], w2_sb[:, m, c * P:(c + 1) * P], h1[:, m, :],
                                                    start=(m == 0 and c == 0), stop=(m == M1 - 1),
                                                    skip_group_check=True)
                    last.then_inc(l2_done, 1)
                if what == "l3":
                    for c in range(M2):
                        pe.wait_ge(l2_out, M2 * k + c + 1)
                        last = nc.tensor.matmul(h_ps[0:1, M2, :], w3_sb[:, c:c + 1], h2[:, c, :],
                                                start=(c == 0), stop=(c == M2 - 1), skip_group_check=True)
                    last.then_inc(l3_done, 1)


def pair_index(i, j):
    return i * FIELDS - i * (i + 1) // 2 + j - i - 1


def kernel(**inputs):
    import concourse.bacc as bacc
    from concourse.bass_utils import run_bass_kernel_spmd

    a = {k: np.asarray(v) for k, v in inputs.items()}
    pairs = a["L0_rec_bilinear_matrices"]
    tiles = np.zeros((TILES, DIM, G, DIM), pairs.dtype)
    w_top1 = a["W_top1"]
    w1 = np.zeros((BLOCKS, P, N1), w_top1.dtype)
    for v, (t, u) in enumerate(UNIT):
        b, r = divmod(v, PER_BLOCK)
        for s in range(tiles_in(v)):
            for jj in range(G):
                i, j = G * u + s, G * t + jj
                if i < j:
                    tiles[TILE0[v] + s, :, jj, :] = pairs[pair_index(i, j)]
                    w1[b, DIM * s + G * r + jj] = w_top1[pair_index(i, j)]
    for q in range(DENSE):
        w1[BLOCKS - 1, DIM * (q // G) + DIM - G + q % G] = w_top1[FIELDS * (FIELDS - 1) // 2 + q]
    tiles = tiles.reshape(TILES, DIM, P)
    mats = np.concatenate([
        tiles[CHUNK0[c]:CHUNK0[c + 1]].reshape(G, CHUNK_Q[c], DIM, P).transpose(0, 2, 1, 3).reshape(P, CHUNK_Q[c] * P)
        for c in range(CHUNKS)], axis=1)
    select = np.zeros((P, SEL_COLS + DIM), np.float32)
    for p in range(P):
        select[p, SEL_COLS + p // DIM] = 1.0
    spread = np.zeros((P, G, 6, DIM), np.float32)
    for p in range(P):
        spread[p, p // DIM, 2:4, p % DIM] = 1.0
    arrays = {
        "ids": a["ids"].reshape(2 * BT, P, FIELDS).transpose(1, 0, 2),
        "dense": a["dense_ctx"],
        "mats": mats,
        "w1": w1.transpose(1, 0, 2),
        "b1": a["b_top1"].reshape(M1, P).T,
        "w2": a["W_top2"].reshape(M1, P, N2).transpose(1, 0, 2),
        "b2": a["b_top2"].reshape(M2, P).T,
        "w3": a["W_top3"].reshape(M2, P).T,
        "ident": np.eye(P, dtype=np.float32),
        "spread_bits": spread.reshape(P, G, 6 * DIM),
        "select": select,
    }
    arrays |= {f"tbl_{f}": a[f"tbl_{f}"] for f in range(FIELDS)}
    arrays = {k: np.ascontiguousarray(v) for k, v in arrays.items()}

    nc = bacc.Bacc("TRN2", target_bir_lowering=False, num_devices=1)
    dram = {k: nc.dram_tensor(k, v.shape, mybir.dt.from_np(v.dtype), kind="ExternalInput").ap() for k, v in arrays.items()}
    out = nc.dram_tensor("out", (BATCH, 1), F32, kind="ExternalOutput").ap()
    tables = [dram.pop(f"tbl_{f}") for f in range(FIELDS)]
    bass_dlrm_tower(nc, tables=tables, out=out, **dram)
    r = run_bass_kernel_spmd(nc, [arrays], core_ids=[0])
    return r.results[0]["out"]
```

```python
from contextlib import ExitStack

import numpy as np

import concourse.bass as bass
from concourse import mybir

F32 = mybir.dt.float32
F32R = mybir.dt.float32r
I32 = mybir.dt.int32
ALU = mybir.AluOpType
ACT = mybir.ActivationFunctionType

P = 128
BATCH, FIELDS, DIM, DENSE = 512, 40, 32, 16
HALF = BATCH // 2
BT = HALF // P
G = P // DIM
GROUPS = FIELDS // G
SETS = 2 * GROUPS
UNITS = GROUPS * (GROUPS + 1) // 2
PER_BLOCK = DIM // G
BLOCKS = -(-UNITS // PER_BLOCK)
N1, N2 = 512, 256
M1, M2 = N1 // P, N2 // P

UNIT = [(t, u) for t in range(GROUPS) for u in range(t + 1)]


def tiles_in(v):
    t, u = UNIT[v]
    return G - 1 if t == u else G


TILE0 = [sum(tiles_in(w) for w in range(v)) for v in range(UNITS + 1)]
CHUNK_Q = [5] + [8] * 6
CHUNKS = len(CHUNK_Q)
CHUNK0 = [G * sum(CHUNK_Q[:c]) for c in range(CHUNKS + 1)]
TILES = CHUNK0[-1]
QMAX = max(CHUNK_Q)
XR_RING, P_RING = 5, 3
LAG = 2
W1_EARLY = 3
LO_BY_SCALAR = [3, 4, 6, 7, 8, 9, 15, 16, 17, 18, 19]
AFTER = {
    "set": [-1, 0, 2, 5, 8, 14, 20, 26, 34, 40, 49, 54, 56, 60, 63, 68, 75, 82, 89, 98],
    "split": [-1, 0, 3, 5, 8, 16, 21, 26, 34, 40, 51, 54, 58, 61, 64, 68, 75, 83, 90, 99],
    "stack0": [-1, 0, 4, 7, 10, 17, 22, 27, 34, 47, 53, 55, 58, 61, 67, 69, 76, 86, 94, 103],
    "stack1": [-1, 0, 4, 7, 13, 17, 22, 30, 36, 47, 54, 55, 58, 61, 67, 73, 80, 87, 96, 103],
    "chunk": [-1, -1, 0, 0, 9, 19, 26],
    "l1a": [10, 18, 46, 54, 57, 58, 59, 67, 73, 84, 92, 101, 109, 111],
    "l1b": [11, 18, 48, 55, 58, 59, 60, 67, 77, 87, 96, 104, 111, 111],
    "l2": [62, 111],
    "l3": [63, 111],
}
SEL_COLS = DIM - G


def first_unit(b):
    return b * PER_BLOCK


def last_unit(b):
    return min((b + 1) * PER_BLOCK, UNITS) - 1


def stacked(n, part):
    first = G * (n % GROUPS) + 2 * part
    return range(first, min(first + 2, FIELDS - 1))


def stacked_by(scalar, n):
    return sum((m in LO_BY_SCALAR) == scalar for m in range(n + 1))


def units_before(n):
    h, t = divmod(n, GROUPS)
    return h * UNITS + t * (t + 1) // 2


def schedule():
    def placed(what, U):
        return [(what, k) for k, after in enumerate(AFTER[what]) if after == U]

    def set_steps(U):
        steps = [s for what in ("set", "split", "stack0", "stack1") for s in placed(what, U)]
        return sorted(steps, key=lambda s: s[1])

    steps = placed("chunk", -1) + set_steps(-1)
    for U in range(2 * UNITS + LAG):
        if U < 2 * UNITS:
            steps.append(("mul", U))
            steps += set_steps(U) + placed("chunk", U)
        if U >= LAG:
            steps.append(("sum", U - LAG))
            h, v = divmod(U - LAG, UNITS)
            if v == last_unit(v // PER_BLOCK):
                steps.append(("z", h * BLOCKS + v // PER_BLOCK))
        for B in range(2 * BLOCKS):
            steps += [(what, B) for what in ("l1a", "l1b") if AFTER[what][B] == U]
        for h in range(2):
            steps += [(what, h) for what in ("l2", "l3") if AFTER[what][h] == U]
    return steps


def bass_dlrm_tower(nc, ids, tables, dense, mats, w1, b1, w2, b2, w3, ident, select, out):
    steps = schedule()
    with ExitStack() as ctx:
        def sb(name, shape, dt=F32):
            return ctx.enter_context(nc.sbuf_tensor(name, shape, dt))

        def ps(name, shape, dt=F32):
            return ctx.enter_context(nc.psum_tensor(name, shape, dt))

        def sem(name):
            return ctx.enter_context(nc.semaphore(name))

        ids_sb = sb("ids_sb", [P, 2 * BT, FIELDS], I32)
        x_rows = sb("x_rows", [P, XR_RING, BT, G, DIM])
        xt = sb("xt", [P, 2, HALF])
        xt_hi = sb("xt_hi", [P, 2, HALF])
        xt_lo = sb("xt_lo", [P, 2, HALF])
        x_stack = sb("x_stack", [P, FIELDS - 1, HALF], F32R)
        m_stack = sb("m_stack", [P, TILE0[UNITS], P], F32R)
        stage = sb("stage", [P, 2, 2, QMAX * P])
        prod = sb("prod", [P, P_RING, G, HALF])
        z_t = sb("z_t", [P, BLOCKS, HALF])
        h1 = sb("h1", [P, M1, HALF])
        y = sb("y", [P, BT])
        w2_sb = sb("w2_sb", [P, M1, N2])
        w3_sb = sb("w3_sb", [P, M2])
        b1_sb = sb("b1_sb", [P, M1])
        b2_sb = sb("b2_sb", [P, M2])
        eye = sb("eye", [P, P])
        sel = sb("sel", [P, SEL_COLS + DIM])
        dense_pad = sb("dense_pad", [P, 2 * BT, G, DIM])
        stage_slots = stage[:].rearrange("p slot kind c -> p slot (kind c)")
        h2 = stage_slots[:, 0, 0:M2 * HALF].rearrange("p (c b) -> p c b", c=M2)
        w1_early = sb("w1_early", [P, W1_EARLY, N1])
        w1_late = stage_slots[:, 1, 0:(BLOCKS - W1_EARLY) * N1].rearrange("p (b n) -> p b n", b=BLOCKS - W1_EARLY)

        y_ps = ps("y_ps", [P, 2, G, HALF])
        z_ps = ps("z_ps", [P, 512])
        t_ps = ps("t_ps", [P, 512])
        h_ps = ps("h_ps", [P, M1, HALF])

        ids_in = sem("ids_in")
        eye_in = sem("eye_in")
        sel_in = sem("sel_in")
        head_in = sem("head_in")
        pad_zeroed = sem("pad_zeroed")
        dense_in = sem("dense_in")
        w1_early_in = sem("w1_early_in")
        w1_late_in = sem("w1_late_in")
        gathered = [sem(f"gathered{k}") for k in range(XR_RING)]
        raw_in = [sem(f"raw_in{k}") for k in range(2)]
        m_hi_done = sem("m_hi_done")
        m_lo_done = sem("m_lo_done")
        m_half_in = [sem(f"m_half_in{c}") for c in range(CHUNKS)]
        m_in_stack = [sem(f"m_in_stack{c}") for c in range(CHUNKS)]
        xt_done = sem("xt_done")
        xt_lo_done = sem("xt_lo_done")
        turned = sem("turned")
        xt_hi_done = sem("xt_hi_done")
        hi_stacked = sem("hi_stacked")
        lo_stacked_v = sem("lo_stacked_v")
        lo_stacked_s = sem("lo_stacked_s")
        y_done = sem("y_done")
        prod_done = sem("prod_done")
        sum_done = sem("sum_done")
        z_out = sem("z_out")
        l1_done = sem("l1_done")
        l1_out = sem("l1_out")
        l2_done = sem("l2_done")
        l2_out = sem("l2_out")
        l3_done = sem("l3_done")
        y_out = sem("y_out")
        stored = sem("stored")
        block = ctx.enter_context(nc.Block())

        def stage_slot(kind, c, dt=F32):
            s = stage[:, c % 2, kind, 0:CHUNK_Q[c] * P]
            return s if dt == F32 else s.bitcast(dt)

        @block.gpsimd
        def _(pool):
            pool.wait_ge(ids_in, 16)
            for n in range(SETS):
                h, t = divmod(n, GROUPS)
                if n >= XR_RING:
                    pool.wait_ge(turned, n - XR_RING + 1)
                for bt in range(BT):
                    for f in range(G):
                        row = bass.IndirectOffsetOnAxis(ap=ids_sb[:, BT * h + bt, G * t + f:G * t + f + 1], axis=0)
                        pool.indirect_dma_start(out=x_rows[:, n % XR_RING, bt, f, :], out_offset=None,
                                                in_=tables[G * t + f], in_offset=row
                                                ).then_inc(gathered[n % XR_RING], 16)

        @block.sync
        def _(sp):
            def load_raw(c):
                q0 = CHUNK0[c] // G
                sp.dma_start(stage_slot(0, c), mats[:, q0 * P:(q0 + CHUNK_Q[c]) * P]).then_inc(raw_in[c % 2], 16)

            sp.dma_start(ids_sb[:], ids).then_inc(ids_in, 16)
            load_raw(0)
            load_raw(1)
            sp.wait_ge(pad_zeroed, 1)
            for c in range(CHUNKS):
                if c == 1:
                    sp.dma_start(w1_early[:], w1[:, 0:W1_EARLY, :]).then_inc(w1_early_in, 16)
                if c == CHUNKS - 1:
                    sp.wait_ge(m_half_in[CHUNKS - 2], 16 * 2 * G)
                    sp.dma_start(w1_late, w1[:, W1_EARLY:BLOCKS, :]).then_inc(w1_late_in, 16)
                sp.wait_ge(m_hi_done, c + 1)
                sp.wait_ge(m_lo_done, c + 1)
                q = CHUNK_Q[c]
                for g in range(G):
                    tile0 = CHUNK0[c] + g * q
                    w = min(q, TILE0[UNITS] - tile0)
                    for row in (0, 1):
                        src = stage_slot(1 - row, c)[g * DIM:(g + 1) * DIM, 0:w * P]
                        dst = m_stack[row * DIM:(row + 1) * DIM, tile0:tile0 + w, :]
                        sp.dma_start(dst.rearrange("p q c -> p (q c)").bitcast(F32), src).then_inc(m_half_in[c], 16)
                sp.wait_ge(m_half_in[c], 16 * 2 * G)
                if c + 2 < CHUNKS:
                    load_raw(c + 2)
                tiles = slice(CHUNK0[c], min(CHUNK0[c + 1], TILE0[UNITS]))
                sp.dma_start(m_stack[2 * DIM:4 * DIM, tiles, :].bitcast(F32),
                             m_stack[0:2 * DIM, tiles, :].bitcast(F32)).then_inc(m_in_stack[c], 16)
            for bt in range(2 * BT):
                sp.dma_start(dense_pad[:, bt, :, DIM - G:DIM], dense[bt * P:(bt + 1) * P, :].rearrange(
                    "p (s q) -> p s q", s=G)).then_inc(dense_in, 16)
            sp.dma_start(w2_sb[:], w2).then_inc(head_in, 16)
            sp.dma_start(w3_sb[:], w3).then_inc(head_in, 16)
            sp.dma_start(b1_sb[:], b1).then_inc(head_in, 16)
            sp.dma_start(b2_sb[:], b2).then_inc(head_in, 16)
            for h in range(2):
                sp.wait_ge(y_out, h + 1)
                sp.dma_start(out[h * HALF:(h + 1) * HALF, :].rearrange("(p bt) o -> p (bt o)", bt=BT),
                             y[:]).then_inc(stored, 16)
            sp.wait_ge(stored, 32)

        @block.scalar
        def _(act):
            act.dma_start(eye[:], ident).then_inc(eye_in, 16)
            act.dma_start(sel[:], select).then_inc(sel_in, 16)
            for what, k in steps:
                if what == "chunk":
                    c = k
                    act.wait_ge(raw_in[c % 2], 16 * (c // 2 + 1))
                    if c >= 2:
                        act.wait_ge(m_half_in[c - 2], 16 * 2 * G)
                    nc.scalar.activation(stage_slot(1, c, F32R), stage_slot(0, c), ACT.Copy).then_inc(m_hi_done, 1)
                if what == "set":
                    n = k
                    act.wait_ge(turned, n + 1)
                    if n >= 2:
                        act.wait_ge(prod_done, units_before(n - 1))
                    nc.scalar.activation(xt[:, n % 2, :], t_ps[:, 0:HALF], ACT.Copy).then_inc(xt_done, 1)
                    nc.scalar.activation(xt_hi[:, n % 2, :].bitcast(F32R), t_ps[:, 0:HALF],
                                         ACT.Copy).then_inc(xt_hi_done, 1)
                if what in ("stack0", "stack1"):
                    n, part = k, int(what[-1])
                    h, t = divmod(n, GROUPS)
                    if h == 1 and part == 0:
                        act.wait_ge(y_done, UNITS - GROUPS + t + 1)
                    for field in stacked(n, part):
                        f = field % G
                        for row in (0, 1):
                            last = nc.scalar.activation(x_stack[row * DIM:(row + 1) * DIM, field, :],
                                                        t_ps[f * DIM:(f + 1) * DIM, 0:HALF], ACT.Copy)
                    if part == 1:
                        last.then_inc(hi_stacked, 1)
                    if n in LO_BY_SCALAR:
                        act.wait_ge(xt_lo_done, n + 1)
                        for field in stacked(n, part):
                            f = field % G
                            for row in (2, 3):
                                last = nc.scalar.activation(x_stack[row * DIM:(row + 1) * DIM, field, :],
                                                            xt_lo[f * DIM:(f + 1) * DIM, n % 2, :], ACT.Copy)
                        if part == 1:
                            last.then_inc(lo_stacked_s, 1)
                if what == "z":
                    h, b = divmod(k, BLOCKS)
                    act.wait_ge(sum_done, h * UNITS + last_unit(b) + 1)
                    if h == 1:
                        act.wait_ge(l1_done, 2 * (b + 1))
                    nc.scalar.activation(z_t[:, b, :], z_ps[:, 0:HALF], ACT.Copy).then_inc(z_out, 1)
                if what == "l1b" and k % BLOCKS == BLOCKS - 1:
                    h = k // BLOCKS
                    act.wait_ge(head_in, 16 * 4)
                    if h == 1:
                        act.wait_ge(l2_done, M2)
                    for m in range(M1):
                        act.wait_ge(l1_done, 2 * (k + 1) - 1 + m // 2)
                        nc.scalar.activation(h1[:, m, :], h_ps[:, m, :], ACT.Relu,
                                             bias=b1_sb[:, m:m + 1]).then_inc(l1_out, 1)
                if what == "l2":
                    if k == 1:
                        act.wait_ge(l3_done, 1)
                    for m in range(M2):
                        act.wait_ge(l2_done, M2 * k + m + 1)
                        nc.scalar.activation(h2[:, m, :], h_ps[:, 2 * m, :], ACT.Relu,
                                             bias=b2_sb[:, m:m + 1]).then_inc(l2_out, 1)
                if what == "l3":
                    act.wait_ge(l3_done, k + 1)
                    if k == 1:
                        act.wait_ge(stored, 16)
                    nc.scalar.activation(y[:], h_ps[:, 1, 0:BT], ACT.Copy).then_inc(y_out, 1)

        @block.vector
        def _(dve):
            nc.vector.memset(dense_pad[:], 0.0).then_inc(pad_zeroed, 1)
            for what, k in steps:
                if what == "chunk":
                    dve.wait_ge(m_hi_done, k + 1)
                    nc.vector.tensor_tensor(stage_slot(0, k, F32R), stage_slot(0, k), stage_slot(1, k),
                                            ALU.subtract).then_inc(m_lo_done, 1)
                if what == "split":
                    n = k
                    dve.wait_ge(xt_done, n + 1)
                    dve.wait_ge(xt_hi_done, n + 1)
                    if n - 2 in LO_BY_SCALAR:
                        dve.wait_ge(lo_stacked_s, stacked_by(True, n - 2))
                    nc.vector.tensor_tensor(xt_lo[:, n % 2, :].bitcast(F32R), xt[:, n % 2, :], xt_hi[:, n % 2, :],
                                            ALU.subtract).then_inc(xt_lo_done, 1)
                if what in ("stack0", "stack1") and k not in LO_BY_SCALAR:
                    n, part = k, int(what[-1])
                    h, t = divmod(n, GROUPS)
                    dve.wait_ge(xt_lo_done, n + 1)
                    if h == 1 and part == 0:
                        dve.wait_ge(y_done, UNITS - GROUPS + t + 1)
                    for field in stacked(n, part):
                        f = field % G
                        for row in (2, 3):
                            last = nc.vector.tensor_copy(x_stack[row * DIM:(row + 1) * DIM, field, :],
                                                         xt_lo[f * DIM:(f + 1) * DIM, n % 2, :])
                    if part == 1:
                        last.then_inc(lo_stacked_v, 1)
                if what == "mul":
                    h, v = divmod(k, UNITS)
                    t, u = UNIT[v]
                    n = h * GROUPS + t
                    w = tiles_in(v)
                    if u == 0:
                        dve.wait_ge(xt_done, n + 1)
                    dve.wait_ge(y_done, k + 1)
                    if k >= P_RING:
                        dve.wait_ge(sum_done, k - P_RING + 1)
                    nc.vector.tensor_tensor(prod[:, k % P_RING, 0:w, :], y_ps[:, k % 2, 0:w, :],
                                            xt[:, n % 2, :].unsqueeze(1).to_broadcast([P, w, HALF]),
                                            ALU.mult).then_inc(prod_done, 1)

        @block.tensor
        def _(pe):
            pe.wait_ge(eye_in, 16)
            chunks_seen = 0
            for what, k in steps:
                if what == "set":
                    n = k
                    pe.wait_ge(gathered[n % XR_RING], 16 * BT * G * (n // XR_RING + 1))
                    if n >= 1:
                        pe.wait_ge(hi_stacked, n)
                    for bt in range(BT):
                        rows = x_rows[:, n % XR_RING, bt, :, :].rearrange("p f d -> p (f d)")
                        last = nc.tensor.transpose(t_ps[:, bt * P:(bt + 1) * P], rows, eye[:])
                    last.then_inc(turned, 1)
                if what == "mul":
                    h, v = divmod(k, UNITS)
                    t, u = UNIT[v]
                    n = h * GROUPS + t
                    while CHUNK0[chunks_seen] < TILE0[v + 1] and chunks_seen < CHUNKS and h == 0:
                        pe.wait_ge(m_in_stack[chunks_seen], 16)
                        chunks_seen += 1
                    if u == t:
                        pe.wait_ge(hi_stacked, n + 1)
                        if n in LO_BY_SCALAR:
                            pe.wait_ge(lo_stacked_s, stacked_by(True, n))
                        else:
                            pe.wait_ge(lo_stacked_v, stacked_by(False, n))
                    if k >= 2:
                        pe.wait_ge(prod_done, k - 1)
                    for s in range(tiles_in(v)):
                        last = nc.tensor.matmul(y_ps[:, k % 2, s, :], m_stack[:, TILE0[v] + s, :],
                                                x_stack[:, G * u + s, :], start=True, stop=True)
                    last.then_inc(y_done, 1)
                if what == "sum":
                    h, v = divmod(k, UNITS)
                    b, r = divmod(v, PER_BLOCK)
                    B = h * BLOCKS + b
                    if k == 0:
                        pe.wait_ge(sel_in, 16)
                    if r == 0 and B >= 1:
                        pe.wait_ge(z_out, B)
                    started = [first_unit(b) + (tiles_in(first_unit(b)) <= s) for s in range(G)]
                    if b == BLOCKS - 1 and r == 0:
                        pe.wait_ge(dense_in, 16 * 2 * BT)
                        for s in range(G):
                            for bt in range(BT):
                                nc.tensor.matmul(z_ps[s * DIM:(s + 1) * DIM, bt * P:(bt + 1) * P],
                                                 dense_pad[:, BT * h + bt, s, :], eye[:], start=(bt == 0),
                                                 stop=False, skip_group_check=True)
                        started = [-1] * G
                    pe.wait_ge(prod_done, k + 1)
                    for s in range(tiles_in(v)):
                        window = sel[:, SEL_COLS - G * r:SEL_COLS - G * r + DIM]
                        last = nc.tensor.matmul(z_ps[s * DIM:(s + 1) * DIM, 0:HALF], window,
                                                prod[:, k % P_RING, s, :], start=(v == started[s]),
                                                stop=(v >= last_unit(b) - 1), skip_group_check=True)
                    last.then_inc(sum_done, 1)
                if what in ("l1a", "l1b"):
                    h, b = divmod(k, BLOCKS)
                    pe.wait_ge(z_out, k + 1)
                    if k == 0:
                        pe.wait_ge(w1_early_in, 16)
                    if k == W1_EARLY:
                        pe.wait_ge(w1_late_in, 16)
                    w1_block = w1_early[:, b, :] if b < W1_EARLY else w1_late[:, b - W1_EARLY, :]
                    if k == BLOCKS:
                        pe.wait_ge(y_out, 1)
                    for m in (0, 1) if what == "l1a" else (2, 3):
                        last = nc.tensor.matmul(h_ps[:, m, :], w1_block[:, m * P:(m + 1) * P], z_t[:, b, :],
                                                start=(b == 0 and m % 2 == 0), stop=(b == BLOCKS - 1),
                                                skip_group_check=True)
                    last.then_inc(l1_done, 1)
                if what == "l2":
                    pe.wait_ge(head_in, 16 * 4)
                    for c in range(M2):
                        for m in range(M1):
                            if c == 0:
                                pe.wait_ge(l1_out, M1 * k + max(m + 1, 2))
                            last = nc.tensor.matmul(h_ps[:, 2 * c, :], w2_sb[:, m, c * P:(c + 1) * P], h1[:, m, :],
                                                    start=(m == 0), stop=(m == M1 - 1))
                        last.then_inc(l2_done, 1)
                if what == "l3":
                    for c in range(M2):
                        pe.wait_ge(l2_out, M2 * k + c + 1)
                        for bt in range(BT):
                            last = nc.tensor.matmul(h_ps[:, 1, bt:bt + 1], h2[:, c, bt * P:(bt + 1) * P],
                                                    w3_sb[:, c:c + 1], start=(c == 0 and bt == 0),
                                                    stop=(c == M2 - 1), skip_group_check=True)
                    last.then_inc(l3_done, 1)


def pair_index(i, j):
    return i * FIELDS - i * (i + 1) // 2 + j - i - 1


def kernel(**inputs):
    import concourse.bacc as bacc
    from concourse.bass_utils import run_bass_kernel_spmd

    a = {k: np.asarray(v) for k, v in inputs.items()}
    pairs = a["L0_rec_bilinear_matrices"]
    tiles = np.zeros((TILES, DIM, G, DIM), pairs.dtype)
    w_top1 = a["W_top1"]
    w1 = np.zeros((BLOCKS, P, N1), w_top1.dtype)
    for v, (t, u) in enumerate(UNIT):
        b, r = divmod(v, PER_BLOCK)
        for s in range(tiles_in(v)):
            for jj in range(G):
                i, j = G * u + s, G * t + jj
                if i < j:
                    tiles[TILE0[v] + s, :, jj, :] = pairs[pair_index(i, j)]
                    w1[b, DIM * s + G * r + jj] = w_top1[pair_index(i, j)]
    for q in range(DENSE):
        w1[BLOCKS - 1, DIM * (q // G) + DIM - G + q % G] = w_top1[FIELDS * (FIELDS - 1) // 2 + q]
    tiles = tiles.reshape(TILES, DIM, P)
    mats = np.concatenate([
        tiles[CHUNK0[c]:CHUNK0[c + 1]].reshape(G, CHUNK_Q[c], DIM, P).transpose(0, 2, 1, 3).reshape(P, CHUNK_Q[c] * P)
        for c in range(CHUNKS)], axis=1)
    select = np.zeros((P, SEL_COLS + DIM), np.float32)
    for p in range(P):
        select[p, SEL_COLS + p // DIM] = 1.0
    arrays = {
        "ids": a["ids"].reshape(2, P, BT, FIELDS).transpose(1, 0, 2, 3).reshape(P, 2 * BT, FIELDS),
        "dense": a["dense_ctx"].reshape(2, P, BT, DENSE).transpose(0, 2, 1, 3).reshape(BATCH, DENSE),
        "mats": mats,
        "w1": w1.transpose(1, 0, 2),
        "b1": a["b_top1"].reshape(M1, P).T,
        "w2": a["W_top2"].reshape(M1, P, N2).transpose(1, 0, 2),
        "b2": a["b_top2"].reshape(M2, P).T,
        "w3": a["W_top3"].reshape(M2, P).T,
        "ident": np.eye(P, dtype=np.float32),
        "select": select,
    }
    arrays |= {f"tbl_{f}": a[f"tbl_{f}"] for f in range(FIELDS)}
    arrays = {k: np.ascontiguousarray(v) for k, v in arrays.items()}

    nc = bacc.Bacc("TRN2", target_bir_lowering=False, num_devices=1)
    dram = {k: nc.dram_tensor(k, v.shape, mybir.dt.from_np(v.dtype), kind="ExternalInput").ap()
            for k, v in arrays.items()}
    out = nc.dram_tensor("out", (BATCH, 1), F32, kind="ExternalOutput").ap()
    tables = [dram.pop(f"tbl_{f}") for f in range(FIELDS)]
    bass_dlrm_tower(nc, tables=tables, out=out, **dram)
    r = run_bass_kernel_spmd(nc, [arrays], core_ids=[0])
    return r.results[0]["out"]
```
